# Optimizing a Trainium2 kernel written in Bass

```python
import numpy as np
import jax
import jax.numpy as jnp

def _softmax(x, axis=-1):
    return jax.nn.softmax(x, axis=axis)

def _gelu(x):
    return jax.nn.gelu(x, approximate=True)

def _silu(x):
    return jax.nn.silu(x)

def _sigmoid(x):
    return jax.nn.sigmoid(x)

def _layernorm(x, axis=-1, eps=1e-05):
    m = jnp.mean(x, axis=axis, keepdims=True)
    v = jnp.var(x, axis=axis, keepdims=True)
    return (x - m) / jnp.sqrt(v + eps)

def _scatter_add(tgt, idx, src, axis=0):
    return tgt.at[idx].add(src)

def _segment_sum(src, seg, n):
    return jax.ops.segment_sum(src, seg, n)
kernel_name = 'mk_dlrm_tower_d1_rec_r8_a98112'

def setup_inputs(seed: int=0):
    np.random.seed(seed)
    _w = jnp.asarray

    def _rec_inputs():
        import jax
        import jax.numpy as jnp
        _tk = jax.random.key(seed)
        ids = jnp.stack([jax.random.randint(jax.random.fold_in(_tk, 200 + f), (2048,), 0, v, jnp.int32) for f, v in enumerate([1000, 1000, 1000, 1000, 1250, 1250, 125000, 1000, 1000, 1000, 1250, 12500, 1000, 1000, 1250, 12500, 1250, 1000, 1250, 1000, 1250, 12500, 1250, 1000, 1000, 12500])], axis=1)
        tbl_0 = 0.05 * jax.random.normal(jax.random.fold_in(_tk, 500 + 0), (1000, 128), jnp.float32)
        tbl_1 = 0.05 * jax.random.normal(jax.random.fold_in(_tk, 500 + 1), (1000, 128), jnp.float32)
        tbl_2 = 0.05 * jax.random.normal(jax.random.fold_in(_tk, 500 + 2), (1000, 128), jnp.float32)
        tbl_3 = 0.05 * jax.random.normal(jax.random.fold_in(_tk, 500 + 3), (1000, 128), jnp.float32)
        tbl_4 = 0.05 * jax.random.normal(jax.random.fold_in(_tk, 500 + 4), (1250, 128), jnp.float32)
        tbl_5 = 0.05 * jax.random.normal(jax.random.fold_in(_tk, 500 + 5), (1250, 128), jnp.float32)
        tbl_6 = 0.05 * jax.random.normal(jax.random.fold_in(_tk, 500 + 6), (125000, 128), jnp.float32)
        tbl_7 = 0.05 * jax.random.normal(jax.random.fold_in(_tk, 500 + 7), (1000, 128), jnp.float32)
        tbl_8 = 0.05 * jax.random.normal(jax.random.fold_in(_tk, 500 + 8), (1000, 128), jnp.float32)
        tbl_9 = 0.05 * jax.random.normal(jax.random.fold_in(_tk, 500 + 9), (1000, 128), jnp.float32)
        tbl_10 = 0.05 * jax.random.normal(jax.random.fold_in(_tk, 500 + 10), (1250, 128), jnp.float32)
        tbl_11 = 0.05 * jax.random.normal(jax.random.fold_in(_tk, 500 + 11), (12500, 128), jnp.float32)
        tbl_12 = 0.05 * jax.random.normal(jax.random.fold_in(_tk, 500 + 12), (1000, 128), jnp.float32)
        tbl_13 = 0.05 * jax.random.normal(jax.random.fold_in(_tk, 500 + 13), (1000, 128), jnp.float32)
        tbl_14 = 0.05 * jax.random.normal(jax.random.fold_in(_tk, 500 + 14), (1250, 128), jnp.float32)
        tbl_15 = 0.05 * jax.random.normal(jax.random.fold_in(_tk, 500 + 15), (12500, 128), jnp.float32)
        tbl_16 = 0.05 * jax.random.normal(jax.random.fold_in(_tk, 500 + 16), (1250, 128), jnp.float32)
        tbl_17 = 0.05 * jax.random.normal(jax.random.fold_in(_tk, 500 + 17), (1000, 128), jnp.float32)
        tbl_18 = 0.05 * jax.random.normal(jax.random.fold_in(_tk, 500 + 18), (1250, 128), jnp.float32)
        tbl_19 = 0.05 * jax.random.normal(jax.random.fold_in(_tk, 500 + 19), (1000, 128), jnp.float32)
        tbl_20 = 0.05 * jax.random.normal(jax.random.fold_in(_tk, 500 + 20), (1250, 128), jnp.float32)
        tbl_21 = 0.05 * jax.random.normal(jax.random.fold_in(_tk, 500 + 21), (12500, 128), jnp.float32)
        tbl_22 = 0.05 * jax.random.normal(jax.random.fold_in(_tk, 500 + 22), (1250, 128), jnp.float32)
        tbl_23 = 0.05 * jax.random.normal(jax.random.fold_in(_tk, 500 + 23), (1000, 128), jnp.float32)
        tbl_24 = 0.05 * jax.random.normal(jax.random.fold_in(_tk, 500 + 24), (1000, 128), jnp.float32)
        tbl_25 = 0.05 * jax.random.normal(jax.random.fold_in(_tk, 500 + 25), (12500, 128), jnp.float32)
        _rk = jax.random.fold_in(_tk, 7)
        r_dense_features = -0.000520686 + 1.00062 * jax.random.normal(jax.random.fold_in(_rk, 101), (2048, 128), jnp.float32)
        W_top1 = 0.0405887 * jax.random.normal(jax.random.fold_in(_tk, 801), (607, 512), jnp.float32)
        W_top2 = 0.0441942 * jax.random.normal(jax.random.fold_in(_tk, 802), (512, 256), jnp.float32)
        W_top3 = 0.0625 * jax.random.normal(jax.random.fold_in(_tk, 803), (256, 1), jnp.float32)
        b_top1 = jnp.zeros((512,), jnp.float32)
        b_top2 = jnp.zeros((256,), jnp.float32)
        return (r_dense_features, ids, tbl_0, tbl_1, tbl_2, tbl_3, tbl_4, tbl_5, tbl_6, tbl_7, tbl_8, tbl_9, tbl_10, tbl_11, tbl_12, tbl_13, tbl_14, tbl_15, tbl_16, tbl_17, tbl_18, tbl_19, tbl_20, tbl_21, tbl_22, tbl_23, tbl_24, tbl_25, W_top1, b_top1, W_top2, b_top2, W_top3)
    r_dense_features, ids, tbl_0, tbl_1, tbl_2, tbl_3, tbl_4, tbl_5, tbl_6, tbl_7, tbl_8, tbl_9, tbl_10, tbl_11, tbl_12, tbl_13, tbl_14, tbl_15, tbl_16, tbl_17, tbl_18, tbl_19, tbl_20, tbl_21, tbl_22, tbl_23, tbl_24, tbl_25, W_top1, b_top1, W_top2, b_top2, W_top3 = _rec_inputs()

    def _L0_rec_setup():
        import jax, jax.numpy as jnp
        import numpy as np
        B, F, D = (2048, 26, 128)
        key = jax.random.key(seed)
        k1, k2 = jax.random.split(key)
        dense_features = jax.random.normal(k1, (B, D), dtype=jnp.float32)
        sparse_features = jax.random.normal(k2, (B, F, D), dtype=jnp.float32)
        return {'dense_features': dense_features, 'sparse_features': sparse_features}
    _L0_rec_all = _L0_rec_setup()
    _L0_rec_in = {k: v for k, v in _L0_rec_all.items() if k in ()}
    del _L0_rec_all
    return {'r_dense_features': r_dense_features, 'ids': ids, 'tbl_0': tbl_0, 'tbl_1': tbl_1, 'tbl_2': tbl_2, 'tbl_3': tbl_3, 'tbl_4': tbl_4, 'tbl_5': tbl_5, 'tbl_6': tbl_6, 'tbl_7': tbl_7, 'tbl_8': tbl_8, 'tbl_9': tbl_9, 'tbl_10': tbl_10, 'tbl_11': tbl_11, 'tbl_12': tbl_12, 'tbl_13': tbl_13, 'tbl_14': tbl_14, 'tbl_15': tbl_15, 'tbl_16': tbl_16, 'tbl_17': tbl_17, 'tbl_18': tbl_18, 'tbl_19': tbl_19, 'tbl_20': tbl_20, 'tbl_21': tbl_21, 'tbl_22': tbl_22, 'tbl_23': tbl_23, 'tbl_24': tbl_24, 'tbl_25': tbl_25, 'W_top1': W_top1, 'b_top1': b_top1, 'W_top2': W_top2, 'b_top2': b_top2, 'W_top3': W_top3}

def reference(r_dense_features, ids, tbl_0, tbl_1, tbl_2, tbl_3, tbl_4, tbl_5, tbl_6, tbl_7, tbl_8, tbl_9, tbl_10, tbl_11, tbl_12, tbl_13, tbl_14, tbl_15, tbl_16, tbl_17, tbl_18, tbl_19, tbl_20, tbl_21, tbl_22, tbl_23, tbl_24, tbl_25, W_top1, b_top1, W_top2, b_top2, W_top3):
    import jax
    import jax.numpy as jnp

    def _L0_rec_ref(dense_features, sparse_features):
        import jax, jax.numpy as jnp
        import numpy as np
        B, F, D = (2048, 26, 128)
        combined = jnp.concatenate([dense_features[:, None, :], sparse_features], axis=1)
        interactions = jnp.einsum('bfd,bgd->bfg', combined, combined)
        iu0, iu1 = np.triu_indices(F + 1, k=1)
        interactions_flat = interactions[:, iu0, iu1]
        return jnp.concatenate([dense_features, interactions_flat], axis=1)
    e = jnp.stack([tbl_0[ids[:, 0]], tbl_1[ids[:, 1]], tbl_2[ids[:, 2]], tbl_3[ids[:, 3]], tbl_4[ids[:, 4]], tbl_5[ids[:, 5]], tbl_6[ids[:, 6]], tbl_7[ids[:, 7]], tbl_8[ids[:, 8]], tbl_9[ids[:, 9]], tbl_10[ids[:, 10]], tbl_11[ids[:, 11]], tbl_12[ids[:, 12]], tbl_13[ids[:, 13]], tbl_14[ids[:, 14]], tbl_15[ids[:, 15]], tbl_16[ids[:, 16]], tbl_17[ids[:, 17]], tbl_18[ids[:, 18]], tbl_19[ids[:, 19]], tbl_20[ids[:, 20]], tbl_21[ids[:, 21]], tbl_22[ids[:, 22]], tbl_23[ids[:, 23]], tbl_24[ids[:, 24]], tbl_25[ids[:, 25]]], axis=1)
    z = _L0_rec_ref(r_dense_features, e)
    z = z.reshape(z.shape[0], -1)
    h = jnp.concatenate([z, r_dense_features], axis=1)
    h = jnp.maximum(h @ W_top1 + b_top1, 0.0)
    h = jnp.maximum(h @ W_top2 + b_top2, 0.0)
    y = h @ W_top3
    return y

_drawn_inputs = setup_inputs


def setup_inputs(seed=0):
    import zlib

    import numpy as np

    out = dict(_drawn_inputs(seed))
    spreads = {'b_top1': (0.0, 0.1), 'b_top2': (0.0, 0.1)}
    factors = {}
    for name, (base, spread) in spreads.items():
        noise = np.random.default_rng([zlib.crc32(name.encode()), seed]).standard_normal(out[name].shape)
        drawn = base * np.exp(spread * noise) if base else spread * noise
        out[name] = jnp.asarray(drawn.astype(out[name].dtype))
    for name, factor in factors.items():
        out[name] = (out[name] * factor).astype(out[name].dtype)
    return out
```

```python
import concourse.bass as bass
from concourse import mybir
from contextlib import ExitStack

P = 128
TABLES = 26
SLOTS = TABLES + 1
D = 128
BATCH = 2048
TILES = BATCH // P
TURNS = TILES // 2
SPAN = 2 * P
QUADS = 4
GROUPS = P // QUADS
COLS = 7
HIDDEN1, HIDDEN2 = 512, 256
CHUNKS1, CHUNKS2 = HIDDEN1 // P, HIDDEN2 // P
PACK = 4
PACKS = -(-SLOTS // PACK)
HALF = GROUPS // 2


def build(nc, dense, ids, tables, w_pairs, w_dense, b1, w2, b2, w3, out):
    fp32, i32 = mybir.dt.float32, mybir.dt.int32
    ACT = mybir.ActivationFunctionType
    ALU = mybir.AluOpType

    with ExitStack() as ctx:
        def sbuf(name, shape, dtype=fp32):
            return ctx.enter_context(nc.sbuf_tensor(name, shape, dtype))

        def psum(name, shape):
            return ctx.enter_context(nc.psum_tensor(name, shape, fp32))

        def sem(name):
            return ctx.enter_context(nc.semaphore(name))

        idx = [sbuf(f"idx{b}", [P, TABLES], i32) for b in range(2)]
        rows = [sbuf(f"rows{b}", [P, SLOTS, D]) for b in range(2)]
        vecT = [sbuf(f"vecT{b}", [P, P, SLOTS]) for b in range(2)]
        denseT = sbuf("denseT", [P, SPAN])
        pairs = sbuf("pairs", [P, COLS, SPAN])
        h1 = sbuf("h1", [P, CHUNKS1, SPAN])
        h2 = sbuf("h2", [P, CHUNKS2, SPAN])
        y = sbuf("y", [1, SPAN])
        wp = sbuf("wp", [P, COLS, HIDDEN1])
        wd2 = sbuf("wd2", [P, 2, HIDDEN1])
        wd = sbuf("wd", [P, HIDDEN1])
        w2s = sbuf("w2s", [P, CHUNKS1, HIDDEN2])
        w3s = sbuf("w3s", [P, CHUNKS2])
        b1s = sbuf("b1s", [P, CHUNKS1])
        b2s = sbuf("b2s", [P, CHUNKS2])
        ident = sbuf("ident", [P, P])

        psT = [psum(f"psT{b}", [P, 512]) for b in range(2)]
        psG = [psum(f"psG{b}", [P, 2, 512]) for b in range(2)]
        psM = [psum(f"psM{b}", [P, 512]) for b in range(2)]

        idx_in = [sem(f"idx_in{b}") for b in range(2)]
        dense_in = [sem(f"dense_in{b}") for b in range(2)]
        gathered = [sem(f"gathered{b}") for b in range(2)]
        gathering = sem("gathering")
        weights_in = sem("weights_in")
        ident_zeroed = sem("ident_zeroed")
        ident_ready = sem("ident_ready")
        packT_ready = sem("packT_ready")
        packT_moved = sem("packT_moved")
        denseT_ready = sem("denseT_ready")
        pairs_zeroed = sem("pairs_zeroed")
        wd_ready = sem("wd_ready")
        gram_ready = sem("gram_ready")
        gram_moved = sem("gram_moved")
        mlp_out = sem("mlp_out")
        mlp_moved = sem("mlp_moved")
        y_stored = sem("y_stored")

        block = ctx.enter_context(nc.Block())
        MLP_STEPS = CHUNKS1 + CHUNKS2 + 1

        @block.sync
        def _(sp):
            with sp.Fori(0, TURNS) as turn:
                for b in range(2):
                    sp.wait_ge(packT_ready, turn * (2 * PACKS) + (b + 1) * PACKS)
                    sp.dma_start(idx[b][:, :], ids[bass.ds(turn * SPAN + b * P, P), :]).then_inc(idx_in[b], 16)
                    sp.dma_start(rows[b][:, 0, :], dense[bass.ds(turn * SPAN + b * P, P), :])\
                        .then_inc(dense_in[b], 16)

        @block.gpsimd
        def _(pool):
            pool.memset(ident[:, :], 0.0).then_inc(ident_zeroed, 1)
            pool.wait_ge(ident_zeroed, 1)
            pool.affine_select(out=ident[:, :], in_=ident[:, :], compare_op=ALU.not_equal, fill=1.0,
                               base=0, pattern=[[-1, P]], channel_multiplier=1).then_inc(ident_ready, 1)
            with pool.Fori(0, TURNS) as turn:
                for b in range(2):
                    pool.wait_ge(idx_in[b], turn * 16 + 16)
                    pool.sem_inc(gathering, 1)
                    for f in range(TABLES):
                        pool.indirect_dma_start(
                            out=rows[b][:, 1 + f, :], out_offset=None, in_=tables[f],
                            in_offset=bass.IndirectOffsetOnAxis(ap=idx[b][:, f:f + 1], axis=0),
                        ).then_inc(gathered[b], 16)

        @block.tensor
        def _(pe):
            pe.sem_inc(packT_ready, 2 * PACKS)
            pe.sem_inc(gram_ready, 2)
            pe.sem_inc(mlp_out, MLP_STEPS)
            pe.wait_ge(ident_ready, 1)
            with pe.Fori(0, TURNS) as turn:
                for b in range(2):
                    pe.wait_ge(gathered[b], turn * (16 * TABLES) + 16 * TABLES)
                    pe.wait_ge(dense_in[b], turn * 16 + 16)
                    for k in range(PACKS):
                        n = min(PACK, SLOTS - k * PACK)
                        pe.wait_ge(packT_moved, turn * (2 * PACKS) + b * PACKS + k + 1)
                        for s in range(n):
                            last = pe.transpose(psT[(b * PACKS + k) % 2][:, s * P:(s + 1) * P],
                                                rows[b][:, k * PACK + s, :], ident[:, :])
                        last.then_inc(packT_ready, 1)
                    pe.wait_ge(packT_moved, turn * (2 * PACKS) + (b + 1) * PACKS + 2)
                    pe.wait_ge(gram_moved, turn * 2 + b + 1)
                    for g in range(GROUPS):
                        for s in range(QUADS):
                            v = vecT[b][:, GROUPS * s + g, :]
                            last = pe.matmul(
                                psG[b][32 * s:32 * s + SLOTS, g // HALF, (g % HALF) * SLOTS:(g % HALF + 1) * SLOTS],
                                v, v, start=True, stop=True)
                    last.then_inc(gram_ready, 1)

                pe.wait_ge(wd_ready, 1)
                pe.wait_ge(denseT_ready, turn * 2 + 2)
                pe.wait_ge(gram_moved, turn * 2 + 4)
                step = 0
                for c in range(CHUNKS1):
                    pe.wait_ge(mlp_moved, turn * MLP_STEPS + max(step + 1, 2))
                    o = psM[c % 2]
                    pe.matmul(o[:, 0:SPAN], wd[:, c * P:(c + 1) * P], denseT[:, :], start=True, stop=False)
                    for j in range(COLS):
                        last = pe.matmul(o[:, 0:SPAN], wp[:, j, c * P:(c + 1) * P], pairs[:, j, :],
                                         start=False, stop=j == COLS - 1)
                    last.then_inc(mlp_out, 1)
                    step += 1
                for c in range(CHUNKS2):
                    pe.wait_ge(mlp_moved, turn * MLP_STEPS + (CHUNKS1 + 2 if c == 0 else step + 1))
                    o = psM[c % 2]
                    for k in range(CHUNKS1):
                        last = pe.matmul(o[:, 0:SPAN], w2s[:, k, c * P:(c + 1) * P], h1[:, k, :],
                                         start=k == 0, stop=k == CHUNKS1 - 1)
                    last.then_inc(mlp_out, 1)
                    step += 1
                pe.wait_ge(mlp_moved, turn * MLP_STEPS + step + 2)
                for k in range(CHUNKS2):
                    last = pe.matmul(psM[0][0:1, 0:SPAN], w3s[:, k:k + 1], h2[:, k, :],
                                     start=k == 0, stop=k == CHUNKS2 - 1)
                last.then_inc(mlp_out, 1)

        @block.vector
        def _(dve):
            dve.memset(pairs[:, :, :], 0.0).then_inc(pairs_zeroed, 1)
            dve.wait_ge(weights_in, 16 * 6)
            dve.tensor_tensor(wd[:, :], wd2[:, 0, :], wd2[:, 1, :], ALU.add).then_inc(wd_ready, 1)
            dve.sem_inc(packT_moved, 2)
            with dve.Fori(0, TURNS) as turn:
                for b in range(2):
                    dve.wait_ge(gram_ready, turn * 2 + b + 1)
                    for k in range(PACKS):
                        n = min(PACK, SLOTS - k * PACK)
                        bank = psT[(b * PACKS + k) % 2]
                        dve.wait_ge(packT_ready, turn * (2 * PACKS) + (2 + b) * PACKS + k + 1)
                        if k == 0:
                            if b == 0:
                                dve.wait_ge(mlp_out, turn * MLP_STEPS + CHUNKS1)
                            dve.tensor_copy(denseT[:, b * P:(b + 1) * P], bank[:, 0:P]).then_inc(denseT_ready, 1)
                        last = dve.tensor_copy(vecT[b][:, :, k * PACK:k * PACK + n],
                                               bank[:, 0:n * P].rearrange("d (s p) -> d p s", s=n))
                        last.then_inc(packT_moved, 1)

        @block.scalar
        def _(act):
            act.dma_start(wp[:, :, :], w_pairs).then_inc(weights_in, 16)
            act.dma_start(wd2[:, :, :], w_dense).then_inc(weights_in, 16)
            act.dma_start(w2s[:, :, :], w2.rearrange("(k p) n -> p k n", p=P)).then_inc(weights_in, 16)
            act.dma_start(w3s[:, :], w3).then_inc(weights_in, 16)
            act.dma_start(b1s[:, :], b1).then_inc(weights_in, 16)
            act.dma_start(b2s[:, :], b2).then_inc(weights_in, 16)
            act.sem_inc(gram_moved, 2)
            act.sem_inc(mlp_moved, 2)
            act.sem_inc(y_stored, 16)
            act.wait_ge(pairs_zeroed, 1)
            act.wait_ge(weights_in, 16 * 6)
            with act.Fori(0, TURNS) as turn:
                for b in range(2):
                    act.wait_ge(gram_ready, turn * 2 + b + 3)
                    for r in range(QUADS):
                        first = 1 + COLS * r
                        n = min(COLS, SLOTS - first)
                        for s in range(QUADS):
                            for half in range(2):
                                at = b * P + GROUPS * s + HALF * half
                                last = act.activation(
                                    pairs[32 * r:32 * r + SLOTS, 0:n, at:at + HALF],
                                    psG[b][32 * s:32 * s + SLOTS, half, 0:HALF * SLOTS]
                                    .rearrange("f (g v) -> f v g", v=SLOTS)[:, first:first + n, :], ACT.Copy)
                    last.then_inc(gram_moved, 1)
                for c in range(CHUNKS1):
                    act.wait_ge(mlp_out, turn * MLP_STEPS + MLP_STEPS + c + 1)
                    last = act.activation(h1[:, c, :], psM[c % 2][:, 0:SPAN], ACT.Relu, bias=b1s[:, c:c + 1])
                    last.then_inc(mlp_moved, 1)
                for c in range(CHUNKS2):
                    act.wait_ge(mlp_out, turn * MLP_STEPS + MLP_STEPS + CHUNKS1 + c + 1)
                    act.activation(h2[:, c, :], psM[c % 2][:, 0:SPAN], ACT.Relu, bias=b2s[:, c:c + 1])\
                        .then_inc(mlp_moved, 1)
                act.wait_ge(mlp_out, turn * MLP_STEPS + 2 * MLP_STEPS)
                act.wait_ge(y_stored, turn * 16 + 16)
                act.activation(y[:, :], psM[0][0:1, 0:SPAN], ACT.Copy).then_inc(mlp_moved, 1)
                act.wait_ge(mlp_moved, turn * MLP_STEPS + MLP_STEPS + 2)
                act.dma_start(out[:, bass.ds(turn * SPAN, SPAN)], y[:, :]).then_inc(y_stored, 16)
            act.wait_ge(y_stored, 16 * TURNS + 16)


def kernel(**inputs):
    import numpy as np
    import concourse.bacc as bacc
    from concourse.bass_utils import run_bass_kernel_spmd

    nc = bacc.Bacc("TRN2", target_bir_lowering=False, num_devices=1)
    arrays, aps = {}, {}

    def give(name, a):
        a = np.ascontiguousarray(a)
        arrays[name] = a
        aps[name] = nc.dram_tensor(name, a.shape, mybir.dt.from_np(a.dtype), kind="ExternalInput").ap()
        return aps[name]

    w1 = np.asarray(inputs["W_top1"])
    n_pairs = SLOTS * (SLOTS - 1) // 2
    w_pairs = np.zeros((P, COLS, HIDDEN1), w1.dtype)
    row = D
    for f in range(SLOTS):
        for g in range(f + 1, SLOTS):
            r, j = divmod(g - 1, COLS)
            w_pairs[32 * r + f, j] = w1[row]
            row += 1
    w_dense = np.stack([w1[:D], w1[D + n_pairs:]], axis=1)
    out = nc.dram_tensor("y_out", (1, BATCH), mybir.dt.float32, kind="ExternalOutput").ap()
    build(nc,
          give("dense", inputs["r_dense_features"]), give("ids", inputs["ids"]),
          [give(f"tbl_{i}", inputs[f"tbl_{i}"]) for i in range(TABLES)],
          give("w_pairs", w_pairs), give("w_dense", w_dense),
          give("b1", np.asarray(inputs["b_top1"]).reshape(CHUNKS1, P).T),
          give("w2", inputs["W_top2"]),
          give("b2", np.asarray(inputs["b_top2"]).reshape(CHUNKS2, P).T),
          give("w3", np.asarray(inputs["W_top3"]).reshape(CHUNKS2, P).T),
          out)
    r = run_bass_kernel_spmd(nc, [arrays], core_ids=[0])
    return r.results[0]["y_out"].reshape(BATCH, 1)
```

```python
import concourse.bass as bass
from concourse import mybir
from contextlib import ExitStack

P = 128
D = 128
BATCH = 2048
TILES = BATCH // P
TURNS = TILES // 2
SPAN = 2 * P
TABLES = 26
SLOTS = TABLES + 1

LOOKUP_TABLES = [0, 1, 2, 3, 7]
LOOKUPS = len(LOOKUP_TABLES)
LOOKUP_ROWS = 1000
BLOCK = 125
BLOCKS = LOOKUP_ROWS // BLOCK
COUPLES = -(-LOOKUPS // 2)
GATHER_TABLES = [t for t in range(TABLES) if t not in LOOKUP_TABLES]
GATHERS = len(GATHER_TABLES)
ROW_SLOTS = 1 + GATHERS

PACK = 4
PACKS = -(-ROW_SLOTS // PACK)

QUADS = 4
GROUPS = P // QUADS
HALF = GROUPS // 2
GRAM_COLS = SLOTS - 1
COLS = 7

HIDDEN1, HIDDEN2 = 512, 256
CHUNKS1, CHUNKS2 = HIDDEN1 // P, HIDDEN2 // P
STEPS = CHUNKS1 + CHUNKS2 + 1


def build(nc, dense, ids, lookup_ids, gather_tables, lookup_tables, w_pairs, w_dense, b1, w2, b2, w3, out):
    fp32, f32r, i32 = mybir.dt.float32, mybir.dt.float32r, mybir.dt.int32
    ACT = mybir.ActivationFunctionType
    ALU = mybir.AluOpType

    with ExitStack() as ctx:
        def sbuf(name, shape, dtype=fp32):
            return ctx.enter_context(nc.sbuf_tensor(name, shape, dtype))

        def psum(name, shape):
            return ctx.enter_context(nc.psum_tensor(name, shape, fp32))

        def sem(name):
            return ctx.enter_context(nc.semaphore(name))

        idx = [sbuf(f"idx{b}", [P, TABLES], i32) for b in range(2)]
        rows = [sbuf(f"rows{b}", [P, ROW_SLOTS, D]) for b in range(2)]
        vecT = [sbuf(f"vecT{b}", [P, P, SLOTS]) for b in range(2)]
        denseT = sbuf("denseT", [P, SPAN])
        pairs = sbuf("pairs", [P, COLS, SPAN])
        h1 = sbuf("h1", [P, CHUNKS1, SPAN])
        h2 = sbuf("h2", [P, CHUNKS2, SPAN])
        y = sbuf("y", [1, BATCH])
        wp = sbuf("wp", [P, COLS, HIDDEN1])
        wd2 = sbuf("wd2", [P, 2, HIDDEN1])
        wd = sbuf("wd", [P, HIDDEN1])
        w2s = sbuf("w2s", [P, CHUNKS1, HIDDEN2])
        w3s = sbuf("w3s", [P, CHUNKS2])
        b1s = sbuf("b1s", [P, CHUNKS1])
        b2s = sbuf("b2s", [P, CHUNKS2])
        ident = sbuf("ident", [P, P])
        table = [sbuf(f"table{n}", [BLOCK, BLOCKS, D]) for n in range(2)]
        high = [sbuf(f"high{q}", [BLOCK, BLOCKS, D], f32r) for q in range(LOOKUPS)]
        low = [sbuf(f"low{q}", [BLOCK, BLOCKS, D], f32r) for q in range(LOOKUPS)]
        onehot = sbuf("onehot", [BLOCK, BLOCKS, LOOKUPS * SPAN], f32r)
        row_number = sbuf("row_number", [P, BLOCKS])
        lids = sbuf("lids", [LOOKUPS, BATCH], i32)
        lidf = sbuf("lidf", [LOOKUPS, BATCH], f32r)
        pick0 = sbuf("pick0", [LOOKUPS, LOOKUPS, P])
        pick = sbuf("pick", [LOOKUPS, LOOKUPS, P], f32r)

        psT = [psum(f"psT{n}", [P, 512]) for n in range(2)]
        psI = [psum(f"psI{n}", [P, 512]) for n in range(2)]
        psG = [psum(f"psG{n}", [P, 512]) for n in range(2)]
        psM = [psum(f"psM{n}", [P, 512]) for n in range(2)]

        idx_in = [sem(f"idx_in{b}") for b in range(2)]
        dense_in = [sem(f"dense_in{b}") for b in range(2)]
        gathered = [sem(f"gathered{b}") for b in range(2)]
        gathering = sem("gathering")
        weights_in = sem("weights_in")
        lids_in = sem("lids_in")
        table_in = [sem(f"table_in{n}") for n in range(2)]
        zeroed = sem("zeroed")
        ident_ready = sem("ident_ready")
        row_number_ready = sem("row_number_ready")
        pick0_ready = sem("pick0_ready")
        pick_ready = sem("pick_ready")
        lidf_ready = sem("lidf_ready")
        high_ready = sem("high_ready")
        low_ready = sem("low_ready")
        pairs_zeroed = sem("pairs_zeroed")
        wd_ready = sem("wd_ready")
        spreading = sem("spreading")
        spread_ids_ready = sem("spread_ids_ready")
        onehot_ready = sem("onehot_ready")
        looked_up = sem("looked_up")
        lookup_moved = sem("lookup_moved")
        pack_ready = sem("pack_ready")
        pack_moved = sem("pack_moved")
        gram_ready = sem("gram_ready")
        gram_moved = sem("gram_moved")
        mlp_ready = sem("mlp_ready")
        mlp_moved = sem("mlp_moved")
        y_stored = sem("y_stored")

        block = ctx.enter_context(nc.Block())

        def couple(q):
            return range(2 * q, min(2 * q + 2, LOOKUPS))

        def bank_of_lookup(q):
            return psT[q % 2]

        def bank_of_pack(b, k):
            return psT[(COUPLES + b * PACKS + k) % 2]

        def pack_slots(k):
            return min(PACK, ROW_SLOTS - k * PACK)

        @block.sync
        def _(sp):
            def load(turn, b):
                sp.dma_start(idx[b][:, :], ids[bass.ds(turn * SPAN + b * P, P), :]).then_inc(idx_in[b], 16)
                sp.dma_start(rows[b][:, 0, :], dense[bass.ds(turn * SPAN + b * P, P), :]).then_inc(dense_in[b], 16)

            load(0, 0)
            sp.dma_start(lids[:, :], lookup_ids).then_inc(lids_in, 16)
            load(0, 1)
            for t in range(LOOKUPS):
                if t >= 2:
                    sp.wait_ge(low_ready, t - 1)
                sp.dma_start(table[t % 2][:, :, :], lookup_tables[t].rearrange("(k p) d -> p k d", p=BLOCK))\
                  .then_inc(table_in[t % 2], 16)
            with sp.Fori(1, TURNS) as turn:
                for b in range(2):
                    sp.wait_ge(pack_ready, turn * (2 * PACKS) - (1 - b) * PACKS)
                    load(turn, b)

        @block.gpsimd
        def _(pool):
            pool.memset(ident[:, :], 0.0).then_inc(zeroed, 1)
            pool.memset(pick0[:, :, :], 0.0).then_inc(zeroed, 1)
            pool.iota(row_number[:, :], pattern=[[BLOCK, BLOCKS]], base=0, channel_multiplier=1,
                      allow_small_or_imprecise_dtypes=True).then_inc(row_number_ready, 1)
            pool.wait_ge(zeroed, 2)
            pool.affine_select(out=pick0[:, :, :], in_=pick0[:, :, :], compare_op=ALU.not_equal, fill=1.0,
                               base=0, pattern=[[-1, LOOKUPS], [0, P]], channel_multiplier=1).then_inc(pick0_ready, 1)
            pool.affine_select(out=ident[:, :], in_=ident[:, :], compare_op=ALU.not_equal, fill=1.0,
                               base=0, pattern=[[-1, P]], channel_multiplier=1).then_inc(ident_ready, 1)

            def gather(b):
                for s, t in enumerate(gather_tables):
                    pool.indirect_dma_start(
                        out=rows[b][:, 1 + s, :], out_offset=None, in_=t,
                        in_offset=bass.IndirectOffsetOnAxis(ap=idx[b][:, GATHER_TABLES[s]:GATHER_TABLES[s] + 1], axis=0),
                    ).then_inc(gathered[b], 16)

            pool.wait_ge(idx_in[0], 16)
            gather(0)
            pool.wait_ge(idx_in[1], 16)
            gather(1)
            with pool.Fori(1, TURNS) as turn:
                for b in range(2):
                    pool.wait_ge(idx_in[b], turn * 16 + 16)
                    pool.sem_inc(gathering, 1)
                    gather(b)

        @block.tensor
        def _(pe):
            def spread_ids(turn, q):
                if q == 2:
                    pe.wait_ge(onehot_ready, turn * COUPLES + 1)
                    pe.sem_inc(spreading, 1)
                for n, t in enumerate(couple(q)):
                    last = pe.matmul(psI[q % 2][:, n * SPAN:(n + 1) * SPAN], pick[:, t, :],
                                     lidf[:, bass.ds(turn * SPAN, SPAN)], start=True, stop=True)
                last.then_inc(spread_ids_ready, 1)

            def look_up(turn, first):
                for q in range(COUPLES):
                    pe.wait_ge(onehot_ready, turn * COUPLES + q + 1)
                    if q >= 2:
                        pe.wait_ge(lookup_moved, turn * COUPLES + q - 1)
                    for n, t in enumerate(couple(q)):
                        if first:
                            pe.wait_ge(low_ready, t + 1)
                        o = bank_of_lookup(q)[:, n * SPAN:(n + 1) * SPAN]
                        for k in range(BLOCKS):
                            hot = onehot[:, k, t * SPAN:(t + 1) * SPAN]
                            pe.matmul(o, high[t][:, k, :], hot, start=k == 0, stop=False)
                            last = pe.matmul(o, low[t][:, k, :], hot, start=False, stop=k == BLOCKS - 1)
                    last.then_inc(looked_up, 1)

            def transpose(turn, b):
                pe.wait_ge(gathered[b], turn * (16 * GATHERS) + 16 * GATHERS)
                pe.wait_ge(dense_in[b], turn * 16 + 16)
                for k in range(PACKS):
                    if b == 0 and k < 2:
                        pe.wait_ge(lookup_moved, turn * COUPLES + COUPLES - 1 + k)
                    elif k >= 2:
                        pe.wait_ge(pack_moved, turn * (2 * PACKS) + b * PACKS + k - 1)
                    for s in range(pack_slots(k)):
                        last = pe.transpose(bank_of_pack(b, k)[:, s * P:(s + 1) * P],
                                            rows[b][:, k * PACK + s, :], ident[:, :])
                    last.then_inc(pack_ready, 1)

            def gram(turn, b, first):
                pe.wait_ge(pack_moved, turn * (2 * PACKS) + (b + 1) * PACKS)
                pe.wait_ge(lookup_moved, turn * COUPLES + COUPLES)
                for half in range(2):
                    if not (first and b == 0):
                        pe.wait_ge(gram_moved, turn * 4 + 2 * b + half - 1)
                    for g in range(HALF):
                        for s in range(QUADS):
                            at = GROUPS * s + HALF * half + g
                            last = pe.matmul(
                                psG[half][32 * s:32 * s + SLOTS, g * GRAM_COLS:(g + 1) * GRAM_COLS],
                                vecT[b][:, at, :], vecT[b][:, at, 1:SLOTS], start=True, stop=True)
                    last.then_inc(gram_ready, 1)

            def layer1(done, grams, lo, hi, first=False):
                pe.wait_ge(gram_moved, grams)
                n = hi - lo
                for c in range(CHUNKS1):
                    if not first:
                        pe.wait_ge(mlp_moved, done + max(c - 1, 0))
                    elif c >= 2:
                        pe.wait_ge(mlp_moved, c - 1)
                    o = psM[c % 2][:, 0:n]
                    pe.matmul(o, wd[:, c * P:(c + 1) * P], denseT[:, lo:hi], start=True, stop=False)
                    for j in range(COLS):
                        last = pe.matmul(o, wp[:, j, c * P:(c + 1) * P], pairs[:, j, lo:hi],
                                         start=False, stop=j == COLS - 1)
                    last.then_inc(mlp_ready, 1)

            def layer2(done, n):
                for c in range(CHUNKS2):
                    pe.wait_ge(mlp_moved, done + CHUNKS1)
                    for k in range(CHUNKS1):
                        last = pe.matmul(psM[c % 2][:, 0:n], w2s[:, k, c * P:(c + 1) * P], h1[:, k, 0:n],
                                         start=k == 0, stop=k == CHUNKS1 - 1)
                    last.then_inc(mlp_ready, 1)

            def layer3(done, n):
                pe.wait_ge(mlp_moved, done + CHUNKS1 + CHUNKS2)
                for k in range(CHUNKS2):
                    last = pe.matmul(psM[0][0:1, 0:n], w3s[:, k:k + 1], h2[:, k, 0:n],
                                     start=k == 0, stop=k == CHUNKS2 - 1)
                last.then_inc(mlp_ready, 1)

            pe.wait_ge(pick_ready, 1)
            pe.wait_ge(lidf_ready, 1)
            for q in range(COUPLES):
                spread_ids(0, q)
            look_up(0, True)
            pe.wait_ge(ident_ready, 1)
            transpose(0, 0)
            spread_ids(1, 0)
            spread_ids(1, 1)
            gram(0, 0, True)
            transpose(0, 1)
            spread_ids(1, 2)
            gram(0, 1, False)
            pe.wait_ge(weights_in, 16 * 6)
            pe.wait_ge(wd_ready, 1)
            pe.wait_ge(pairs_zeroed, 1)

            with pe.Fori(1, TURNS - 1) as turn:
                done = (turn - 1) * STEPS
                look_up(turn, False)
                transpose(turn, 0)
                spread_ids(turn + 1, 0)
                spread_ids(turn + 1, 1)
                layer1(done, turn * 4, 0, SPAN)
                gram(turn, 0, False)
                transpose(turn, 1)
                spread_ids(turn + 1, 2)
                layer2(done, SPAN)
                gram(turn, 1, False)
                layer3(done, SPAN)

            last_turn = TURNS - 1
            done = (last_turn - 1) * STEPS
            look_up(last_turn, False)
            transpose(last_turn, 0)
            layer1(done, last_turn * 4, 0, SPAN)
            gram(last_turn, 0, False)
            layer2(done, SPAN)
            layer3(done, SPAN)
            layer1(done + STEPS, last_turn * 4 + 2, 0, P)
            layer2(done + STEPS, P)
            layer3(done + STEPS, P)
            transpose(last_turn, 1)
            gram(last_turn, 1, False)
            layer1(done + 2 * STEPS, last_turn * 4 + 4, P, SPAN)
            layer2(done + 2 * STEPS, P)
            layer3(done + 2 * STEPS, P)

        @block.vector
        def _(dve):
            def pack(turn, b, first):
                if not first:
                    dve.wait_ge(gram_moved, turn * 4 - 2 + 2 * b)
                for k in range(PACKS):
                    n = pack_slots(k)
                    dve.wait_ge(pack_ready, turn * (2 * PACKS) + b * PACKS + k + 1)
                    dve.tensor_copy(vecT[b][:, :, k * PACK:k * PACK + n],
                                    bank_of_pack(b, k)[:, 0:n * P].rearrange("d (s p) -> d p s", s=n))\
                       .then_inc(pack_moved, 1)

            def make_onehot(turn, q):
                n = len(couple(q)) * SPAN
                dve.wait_ge(spread_ids_ready, turn * COUPLES + q + 1)
                for k in range(BLOCKS):
                    last = dve.tensor_scalar(onehot[:, k, 2 * q * SPAN:2 * q * SPAN + n], psI[q % 2][0:BLOCK, 0:n],
                                             row_number[0:BLOCK, k:k + 1], None, ALU.is_equal)
                last.then_inc(onehot_ready, 1)

            dve.memset(pairs[:, :, :], 0.0).then_inc(pairs_zeroed, 1)
            dve.wait_ge(pick0_ready, 1)
            dve.tensor_copy(pick[:, :, :], pick0[:, :, :]).then_inc(pick_ready, 1)
            dve.wait_ge(row_number_ready, 1)
            for q in range(COUPLES):
                make_onehot(0, q)
                for t in couple(q):
                    dve.wait_ge(high_ready, t + 1)
                    dve.tensor_tensor(low[t][:, :, :], table[t % 2][:, :, :], high[t][:, :, :].bitcast(fp32),
                                      ALU.subtract).then_inc(low_ready, 1)
            dve.wait_ge(weights_in, 16 * 6)
            dve.tensor_tensor(wd[:, :], wd2[:, 0, :], wd2[:, 1, :], ALU.add).then_inc(wd_ready, 1)
            pack(0, 0, True)
            make_onehot(1, 0)
            make_onehot(1, 1)
            pack(0, 1, True)
            make_onehot(1, 2)
            with dve.Fori(1, TURNS - 1) as turn:
                pack(turn, 0, False)
                make_onehot(turn + 1, 0)
                make_onehot(turn + 1, 1)
                pack(turn, 1, False)
                make_onehot(turn + 1, 2)
            pack(TURNS - 1, 0, False)
            pack(TURNS - 1, 1, False)

        @block.scalar
        def _(act):
            def move_lookups(turn):
                for q in range(COUPLES):
                    act.wait_ge(looked_up, turn * COUPLES + q + 1)
                    n = len(couple(q))
                    slot = ROW_SLOTS + 2 * q
                    for b in range(2):
                        last = act.activation(
                            vecT[b][:, :, slot:slot + n],
                            bank_of_lookup(q)[:, 0:n * SPAN]
                            .rearrange("d (s b p) -> d b p s", s=n, b=2)[:, b, :, :], ACT.Copy)
                    last.then_inc(lookup_moved, 1)

            def spread(turn, b):
                for half in range(2):
                    act.wait_ge(gram_ready, turn * 4 + 2 * b + half + 1)
                    if half == 0:
                        act.activation(denseT[:, b * P:(b + 1) * P], vecT[b][:, :, 0], ACT.Copy)
                    for r in range(QUADS):
                        n = min(COLS, GRAM_COLS - COLS * r)
                        for s in range(QUADS):
                            at = b * P + GROUPS * s + HALF * half
                            last = act.activation(
                                pairs[32 * r:32 * r + SLOTS, 0:n, at:at + HALF],
                                psG[half][32 * s:32 * s + SLOTS, 0:HALF * GRAM_COLS]
                                .rearrange("f (g v) -> f v g", v=GRAM_COLS)[:, COLS * r:COLS * r + n, :], ACT.Copy)
                    last.then_inc(gram_moved, 1)

            def relu1(done, n):
                for c in range(CHUNKS1):
                    act.wait_ge(mlp_ready, done + c + 1)
                    act.activation(h1[:, c, 0:n], psM[c % 2][:, 0:n], ACT.Relu, bias=b1s[:, c:c + 1])\
                       .then_inc(mlp_moved, 1)

            def relu2(done, n):
                for c in range(CHUNKS2):
                    act.wait_ge(mlp_ready, done + CHUNKS1 + c + 1)
                    act.activation(h2[:, c, 0:n], psM[c % 2][:, 0:n], ACT.Relu, bias=b2s[:, c:c + 1])\
                       .then_inc(mlp_moved, 1)

            def keep_y(done, at, n):
                act.wait_ge(mlp_ready, done + STEPS)
                act.activation(y[:, bass.ds(at, n)], psM[0][0:1, 0:n], ACT.Copy).then_inc(mlp_moved, 1)

            act.dma_start(wd2[:, :, :], w_dense).then_inc(weights_in, 16)
            act.dma_start(wp[:, :, :], w_pairs).then_inc(weights_in, 16)
            act.dma_start(w2s[:, :, :], w2.rearrange("(k p) n -> p k n", p=P)).then_inc(weights_in, 16)
            act.dma_start(w3s[:, :], w3).then_inc(weights_in, 16)
            act.dma_start(b1s[:, :], b1).then_inc(weights_in, 16)
            act.dma_start(b2s[:, :], b2).then_inc(weights_in, 16)
            act.wait_ge(lids_in, 16)
            act.activation(lidf[:, :], lids[:, :], ACT.Copy).then_inc(lidf_ready, 1)
            for t in range(LOOKUPS):
                act.wait_ge(table_in[t % 2], 16 * (t // 2 + 1))
                act.activation(high[t][:, :, :], table[t % 2][:, :, :], ACT.Copy).then_inc(high_ready, 1)
            move_lookups(0)
            act.wait_ge(pairs_zeroed, 1)
            act.wait_ge(weights_in, 16 * 6)
            spread(0, 0)
            spread(0, 1)
            with act.Fori(1, TURNS - 1) as turn:
                done = (turn - 1) * STEPS
                move_lookups(turn)
                relu1(done, SPAN)
                spread(turn, 0)
                relu2(done, SPAN)
                spread(turn, 1)
                keep_y(done, (turn - 1) * SPAN, SPAN)
            last_turn = TURNS - 1
            done = (last_turn - 1) * STEPS
            move_lookups(last_turn)
            relu1(done, SPAN)
            spread(last_turn, 0)
            relu2(done, SPAN)
            keep_y(done, (last_turn - 1) * SPAN, SPAN)
            for b in range(2):
                if b:
                    spread(last_turn, 1)
                relu1(done + (b + 1) * STEPS, P)
                relu2(done + (b + 1) * STEPS, P)
                keep_y(done + (b + 1) * STEPS, last_turn * SPAN + b * P, P)
            act.wait_ge(mlp_moved, (TURNS + 1) * STEPS)
            act.dma_start(out, y[:, :]).then_inc(y_stored, 16)
            act.wait_ge(y_stored, 16)


def kernel(**inputs):
    import numpy as np
    import concourse.bacc as bacc
    from concourse.bass_utils import run_bass_kernel_spmd

    nc = bacc.Bacc("TRN2", target_bir_lowering=False, num_devices=1)
    arrays = {}

    def give(name, a):
        a = np.ascontiguousarray(a)
        arrays[name] = a
        return nc.dram_tensor(name, a.shape, mybir.dt.from_np(a.dtype), kind="ExternalInput").ap()

    vector_of_slot = [0] + [1 + t for t in GATHER_TABLES + LOOKUP_TABLES]
    w1 = np.asarray(inputs["W_top1"])
    n_pairs = SLOTS * (SLOTS - 1) // 2
    row_of_pair = {}
    for f in range(SLOTS):
        for g in range(f + 1, SLOTS):
            row_of_pair[f, g] = D + len(row_of_pair)
    w_pairs = np.zeros((P, COLS, HIDDEN1), w1.dtype)
    for f in range(SLOTS):
        for g in range(f + 1, SLOTS):
            r, j = divmod(g - 1, COLS)
            u, v = sorted((vector_of_slot[f], vector_of_slot[g]))
            w_pairs[32 * r + f, j] = w1[row_of_pair[u, v]]
    w_dense = np.stack([w1[:D], w1[D + n_pairs:]], axis=1)
    ids = np.asarray(inputs["ids"])
    out = nc.dram_tensor("y_out", (1, BATCH), mybir.dt.float32, kind="ExternalOutput").ap()
    build(nc,
          give("dense", inputs["r_dense_features"]), give("ids", ids),
          give("lookup_ids", ids[:, LOOKUP_TABLES].T),
          [give(f"tbl_{t}", inputs[f"tbl_{t}"]) for t in GATHER_TABLES],
          [give(f"tbl_{t}", inputs[f"tbl_{t}"]) for t in LOOKUP_TABLES],
          give("w_pairs", w_pairs), give("w_dense", w_dense),
          give("b1", np.asarray(inputs["b_top1"]).reshape(CHUNKS1, P).T),
          give("w2", inputs["W_top2"]),
          give("b2", np.asarray(inputs["b_top2"]).reshape(CHUNKS2, P).T),
          give("w3", np.asarray(inputs["W_top3"]).reshape(CHUNKS2, P).T),
          out)
    r = run_bass_kernel_spmd(nc, [arrays], core_ids=[0])
    return r.results[0]["y_out"].reshape(BATCH, 1)
```

```python
import concourse.bass as bass
from concourse import mybir
from contextlib import ExitStack

P = 128
D = 128
BATCH = 2048
TILES = BATCH // P
TURNS = TILES // 2
SPAN = 2 * P
TABLES = 26
SLOTS = TABLES + 1
TWICE = 4
PLACES = SLOTS + TWICE

LOOKUP_TABLES = [0, 1, 2, 3, 7, 8, 9]
LOOKUPS = len(LOOKUP_TABLES)
LOOKUP_ROWS = 1000
BLOCK = 125
BLOCKS = LOOKUP_ROWS // BLOCK
COUPLES = -(-LOOKUPS // 2)
HOTS = 4
HOT_WAIT = [LOOKUPS - max(u for u in range(LOOKUPS) if u % HOTS == t) for t in range(HOTS)]
HOT_WAIT = [w + t for t, w in enumerate(HOT_WAIT)] + [HOTS] * (LOOKUPS - HOTS)
GATHER_TABLES = [t for t in range(TABLES) if t not in LOOKUP_TABLES]
GATHERS = len(GATHER_TABLES)
ROW_SLOTS = 1 + GATHERS

PACK = 4
PACKS = -(-ROW_SLOTS // PACK)

QUADS = 4
GROUPS = P // QUADS
HALF = GROUPS // 2
ROWS = P // QUADS
TOP = ROWS // 2
COLS = 5
TERMS = COLS + 1

WHOLE_MOVES = [(2, 0, 0, 1, 5, PLACES), (3, 0, 5, 1, 2, PLACES), (3, 2, 23, 1, 3, PLACES),
               (0, 0, 13, 1, 5, PLACES), (1, 0, 18, 1, 5, PLACES)]
TOP_MOVES = [(3, 0, 12, 14, 2, TOP), (2, 0, 7, 1, 5, TOP)]
LAST_MOVE = (3, 1, 5, 1, 2, 6)


def pair_places():
    place = {}
    for r, to, col, step, count, rows in WHOLE_MOVES + TOP_MOVES + [LAST_MOVE]:
        for n in range(count):
            for p in range(rows):
                place[ROWS * r + p, to + n] = (p % SLOTS, col + n * step)
    of_pair = {}
    for at, (f, g) in place.items():
        if f != g:
            of_pair[min(f, g), max(f, g)] = at
    assert len(of_pair) == SLOTS * (SLOTS - 1) // 2
    return of_pair


HIDDEN1, HIDDEN2 = 512, 256
CHUNKS1, CHUNKS2 = HIDDEN1 // P, HIDDEN2 // P
STEPS = CHUNKS1 + CHUNKS2 + 1

WIDTH = BLOCKS * D
ITEMS = LOOKUPS + TERMS
assert TWICE == PACK and LOOKUPS * WIDTH <= SPAN * PLACES

T_PACKS = [[2, 3], [2]]
M_PACK = ("pack", 1, 3)
BANK_ORDER = ([("lookup", t) for t in range(HOTS)] + [("pack", 0, k) for k in T_PACKS[0]]
              + [("lookup", t) for t in range(HOTS, LOOKUPS)] + [("pack", 1, k) for k in T_PACKS[1]])
assert len(BANK_ORDER) % 2 == 0 and COUPLES % 2 == 0


def build(nc, dense, ids, lookup_ids, gather_tables, lookup_tables, w_terms, b1, w2, b2, w3, out):
    fp32, f32r, i32 = mybir.dt.float32, mybir.dt.float32r, mybir.dt.int32
    ACT = mybir.ActivationFunctionType
    ALU = mybir.AluOpType

    with ExitStack() as ctx:
        def sbuf(name, shape, dtype=fp32):
            return ctx.enter_context(nc.sbuf_tensor(name, shape, dtype))

        def psum(name, shape):
            return ctx.enter_context(nc.psum_tensor(name, shape, fp32))

        def sem(name):
            return ctx.enter_context(nc.semaphore(name))

        idx = [sbuf(f"idx{b}", [P, TABLES], i32) for b in range(2)]
        rows = [sbuf(f"rows{b}", [P, ROW_SLOTS, D]) for b in range(2)]
        vecT = sbuf("vecT", [P, SPAN, PLACES])
        terms_high = sbuf("terms_high", [P, TERMS, SPAN], f32r)
        terms_low = sbuf("terms_low", [P, TERMS, SPAN], f32r)
        h2 = sbuf("h2", [P, CHUNKS2, SPAN])
        y = sbuf("y", [1, SPAN])
        w1_high = sbuf("w1_high", [P, TERMS, HIDDEN1], f32r)
        w1_low = sbuf("w1_low", [P, TERMS, HIDDEN1], f32r)
        w_dense = sbuf("w_dense", [P, HIDDEN1])
        w2s = sbuf("w2s", [P, CHUNKS1, HIDDEN2])
        w3s = sbuf("w3s", [P, CHUNKS2])
        b1s = sbuf("b1s", [P, CHUNKS1])
        b2s = sbuf("b2s", [P, CHUNKS2])
        ident = sbuf("ident", [P, P])
        table_high = [sbuf(f"table_high{t}", [BLOCK, BLOCKS, D], f32r) for t in range(LOOKUPS)]
        table_low = [sbuf(f"table_low{t}", [BLOCK, BLOCKS, D], f32r) for t in range(LOOKUPS)]
        onehot = [sbuf(f"onehot{n}", [BLOCK, BLOCKS, SPAN], f32r) for n in range(HOTS)]
        row_number = sbuf("row_number", [P, BLOCKS])
        lids = sbuf("lids", [LOOKUPS, SPAN], i32)
        lidf = sbuf("lidf", [LOOKUPS, SPAN], f32r)
        pick = sbuf("pick", [LOOKUPS, LOOKUPS, P], f32r)
        terms = sbuf("terms", [P, TERMS, P])
        h1 = sbuf("h1", [P, CHUNKS1, SPAN])
        w_room = sbuf("w_room", [P, 3, HIDDEN1])

        psT = [psum(f"psT{n}", [P, 512]) for n in range(2)]
        psI = [psum(f"psI{n}", [P, 512]) for n in range(2)]
        psG = [psum(f"psG{n}", [P, 512]) for n in range(2)]
        psM = [psum(f"psM{n}", [P, 512]) for n in range(2)]

        idx_in = [sem(f"idx_in{b}") for b in range(2)]
        dense_in = [sem(f"dense_in{b}") for b in range(2)]
        gathered = [sem(f"gathered{b}") for b in range(2)]
        gathering = sem("gathering")
        constants_in = sem("constants_in")
        lids_in = sem("lids_in")
        lids_taken = sem("lids_taken")
        item_in = [sem(f"item_in{n}") for n in range(ITEMS)]
        ident_zeroed = sem("ident_zeroed")
        ident_ready = sem("ident_ready")
        row_number_ready = sem("row_number_ready")
        pick_ready = sem("pick_ready")
        w_dense_ready = sem("w_dense_ready")
        item_high = sem("item_high")
        item_low = sem("item_low")
        terms_zeroed = sem("terms_zeroed")
        vector_whole_moved = sem("vector_whole_moved")
        vector_tops_moved = sem("vector_tops_moved")
        whole_moved = sem("whole_moved")
        tops_moved = sem("tops_moved")
        ids_spread = sem("ids_spread")
        onehot_ready = sem("onehot_ready")
        looked_up = sem("looked_up")
        lookup_moved = sem("lookup_moved")
        pack_ready = sem("pack_ready")
        packs_moved = [sem("even_packs_moved"), sem("odd_packs_moved")]
        gram_ready = sem("gram_ready")
        gram_moved = sem("gram_moved")
        terms_high_ready = sem("terms_high_ready")
        terms_low_ready = sem("terms_low_ready")
        mlp_ready = sem("mlp_ready")
        mlp_moved = sem("mlp_moved")
        y_stored = sem("y_stored")

        def spread_moves(move, half, moves):
            for r, to, col, step, count, rows in moves:
                for s in range(QUADS):
                    at = GROUPS * s + HALF * half
                    gram = psG[half][ROWS * s:ROWS * s + rows, 0:HALF * SLOTS]\
                        .rearrange("f (g v) -> f v g", v=SLOTS)
                    last = move(terms[ROWS * r:ROWS * r + rows, to:to + count, at:at + HALF],
                                gram[:, col:col + (count - 1) * step + 1:step, :])
            return last

        LAST_BANKS = psI + psT

        block = ctx.enter_context(nc.Block())

        def bank(*use):
            if use in BANK_ORDER:
                return psT[BANK_ORDER.index(use) % 2]
            if use == M_PACK:
                return psM[1]
            return psG[use[2] % 2]

        def pack_slots(k):
            return min(PACK, ROW_SLOTS - k * PACK)

        def item(n):
            flat = "p j n -> p (j n)"
            if n < LOOKUPS:
                raw = vecT[0:BLOCK, :, :].rearrange("p s v -> p (s v)")[:, n * WIDTH:(n + 1) * WIDTH]
                return raw, table_high[n][:, :, :].rearrange(flat), table_low[n][:, :, :].rearrange(flat)
            w = n - LOOKUPS
            return w_dense[:, :] if w == COLS else w_places[w], w1_high[:, w, :], w1_low[:, w, :]

        w_places = [h1[:, 0:CHUNKS1 // 2, :].rearrange("p c s -> p (c s)"),
                    h1[:, CHUNKS1 // 2:CHUNKS1, :].rearrange("p c s -> p (c s)"),
                    h2[:, :, :].rearrange("p c s -> p (c s)"), w_room[:, 0, :], w_room[:, 1, :], w_room[:, 2, :]]

        @block.sync
        def _(sp):
            def load_idx(turn, b):
                sp.dma_start(idx[b][:, :], ids[bass.ds(turn * SPAN + b * P, P), :]).then_inc(idx_in[b], 16)

            def load_dense(turn, b):
                sp.dma_start(rows[b][:, 0, :], dense[bass.ds(turn * SPAN + b * P, P), :]).then_inc(dense_in[b], 16)

            def load_lids(turn):
                sp.dma_start(lids[:, :], lookup_ids[:, bass.ds(turn * SPAN, SPAN)]).then_inc(lids_in, 16)

            load_idx(0, 0)
            load_lids(0)
            load_idx(0, 1)
            load_dense(0, 0)
            load_dense(0, 1)
            for n in range(ITEMS):
                if n < LOOKUPS:
                    src = lookup_tables[n].rearrange("(k p) d -> p k d", p=BLOCK)
                    sp.dma_start(item(n)[0].rearrange("p (k d) -> p k d", k=BLOCKS), src).then_inc(item_in[n], 16)
                else:
                    w = n - LOOKUPS
                    if w == COLS:
                        sp.dma_start(w_dense[:, :], w_terms[:, w, :]).then_inc(item_in[n], 16)
                        w += 1
                    sp.dma_start(w_places[min(w, COLS)], w_terms[:, w, :]).then_inc(item_in[n], 16)
            sp.wait_ge(lids_taken, 1)
            load_lids(1)
            sp.wait_ge(gathered[0], 16 * GATHERS)
            load_idx(1, 0)

            def loads(turn, more, first=False):
                for b in range(2):
                    if not (b == 0 and first):
                        sp.wait_ge(gathered[b], turn * (16 * GATHERS))
                        load_idx(turn, b)
                    sp.wait_ge(pack_ready, turn * (2 * PACKS) - (1 - b) * PACKS)
                    load_dense(turn, b)
                    if b == 0 and more:
                        sp.wait_ge(lids_taken, turn + 1)
                        load_lids(turn + 1)

            loads(1, True, True)
            with sp.Fori(2, TURNS - 1) as turn:
                loads(turn, True)
            loads(TURNS - 1, False)

        @block.gpsimd
        def _(pool):
            def gather(b):
                for s, t in enumerate(gather_tables):
                    f = GATHER_TABLES[s]
                    pool.indirect_dma_start(
                        out=rows[b][:, 1 + s, :], out_offset=None, in_=t,
                        in_offset=bass.IndirectOffsetOnAxis(ap=idx[b][:, f:f + 1], axis=0),
                    ).then_inc(gathered[b], 16)

            pool.memset(ident[:, :], 0.0).then_inc(ident_zeroed, 1)
            pool.iota(row_number[:, :], pattern=[[BLOCK, BLOCKS]], base=0, channel_multiplier=1,
                      allow_small_or_imprecise_dtypes=True).then_inc(row_number_ready, 1)
            pool.memset(terms[:, :, :], 0.0).then_inc(terms_zeroed, 1)
            pool.wait_ge(ident_zeroed, 1)
            pool.affine_select(out=ident[:, :], in_=ident[:, :], compare_op=ALU.not_equal, fill=1.0,
                               base=0, pattern=[[-1, P]], channel_multiplier=1).then_inc(ident_ready, 1)
            for b in range(2):
                pool.wait_ge(idx_in[b], 16)
                gather(b)
            with pool.Fori(1, TURNS) as turn:
                for b in range(2):
                    pool.wait_ge(idx_in[b], turn * 16 + 16)
                    pool.wait_ge(pack_ready, turn * (2 * PACKS) - (1 - b) * PACKS)
                    pool.sem_inc(gathering, 1)
                    gather(b)

        @block.tensor
        def _(pe):
            def spread_ids(turn, q, first=False):
                if q >= 2:
                    pe.wait_ge(onehot_ready, turn * LOOKUPS + 2 * (q - 1))
                elif not first:
                    pe.wait_ge(onehot_ready, turn * LOOKUPS - (LOOKUPS - 2 * (COUPLES - 1) if q == 0 else 0))
                for n in range(min(2, LOOKUPS - 2 * q)):
                    last = pe.matmul(psI[q % 2][:, n * SPAN:(n + 1) * SPAN], pick[:, 2 * q + n, :],
                                     lidf[:, :], start=True, stop=True)
                last.then_inc(ids_spread, 1)

            def wait_packs(turn, b, n):
                odd = (n - 1) % 2
                each = PACKS // 2 if odd else (PACKS + 1) // 2
                pe.wait_ge(packs_moved[odd], turn * (2 * each) + b * each + (n + 1) // 2)

            def bank_empty(turn, *use, first=False):
                if use not in BANK_ORDER:
                    b, k = use[1:]
                    if use == M_PACK:
                        if not first:
                            pe.wait_ge(mlp_moved, (turn - 1) * STEPS + CHUNKS1)
                    elif k >= PACK:
                        wait_packs(turn, b, k - PACK + 1)
                    elif b == 1 or not first:
                        pe.wait_ge(gram_moved, turn * 4 + 2 * b - 1 + k % 2)
                    return
                at = BANK_ORDER.index(use) - 2
                if at >= 0:
                    before = BANK_ORDER[at]
                    if before[0] == "lookup":
                        pe.wait_ge(lookup_moved, turn * LOOKUPS + before[1] + 1)
                    else:
                        wait_packs(turn, before[1], before[2] + 1)

            def look_up(turn, t, first=False):
                bank_empty(turn, "lookup", t)
                if first:
                    pe.wait_ge(item_low, t + 1)
                pe.wait_ge(onehot_ready, turn * LOOKUPS + t + 1)
                o = bank("lookup", t)[:, 0:SPAN]
                for k in range(BLOCKS):
                    hot = onehot[t % HOTS][:, k, :]
                    pe.matmul(o, table_high[t][:, k, :], hot, start=k == 0, stop=False)
                    last = pe.matmul(o, table_low[t][:, k, :], hot, start=False, stop=k == BLOCKS - 1)
                last.then_inc(looked_up, 1)

            def transpose(turn, b, first=False):
                pe.wait_ge(gathered[b], turn * (16 * GATHERS) + 16 * GATHERS)
                pe.wait_ge(dense_in[b], turn * 16 + 16)
                for k in range(PACKS):
                    bank_empty(turn, "pack", b, k, first=first)
                    for s in range(pack_slots(k)):
                        last = pe.transpose(bank("pack", b, k)[:, s * P:(s + 1) * P],
                                            rows[b][:, k * PACK + s, :], ident[:, :])
                    last.then_inc(pack_ready, 1)

            def gram(turn, b, half):
                if half == 0:
                    wait_packs(turn, b, PACKS - 1)
                    wait_packs(turn, b, PACKS)
                    pe.wait_ge(lookup_moved, turn * LOOKUPS + LOOKUPS)
                for g in range(HALF):
                    for s in range(QUADS):
                        at = b * P + GROUPS * s + HALF * half + g
                        last = pe.matmul(
                            psG[half][ROWS * s:ROWS * s + PLACES, g * SLOTS:(g + 1) * SLOTS],
                            vecT[:, at, :], vecT[:, at, 0:SLOTS], start=True, stop=True)
                last.then_inc(gram_ready, 1)

            def layer1_high(m, c, bank=None):
                if c == 0:
                    pe.wait_ge(terms_high_ready, m * 2 + 2)
                if c >= 2 and bank is None:
                    pe.wait_ge(mlp_moved, m * STEPS + c - 1)
                o = (psM[c % 2] if bank is None else bank)[:, 0:SPAN]
                w = slice(c * P, (c + 1) * P)
                for j in range(TERMS):
                    pe.matmul(o, w1_high[:, j, w], terms_high[:, j, :], start=j == 0, stop=False)
                    pe.matmul(o, w1_low[:, j, w], terms_high[:, j, :], start=False, stop=False)

            def layer1_low(m, c, bank=None):
                if c == 0:
                    pe.wait_ge(terms_low_ready, m * 2 + 2)
                o = (psM[c % 2] if bank is None else bank)[:, 0:SPAN]
                w = slice(c * P, (c + 1) * P)
                for j in range(TERMS):
                    last = pe.matmul(o, w1_high[:, j, w], terms_low[:, j, :], start=False, stop=j == TERMS - 1)
                last.then_inc(mlp_ready, 1)

            def layer1(m, c, bank=None):
                layer1_high(m, c, bank)
                layer1_low(m, c, bank)

            def layer2(m, c, chunks=range(CHUNKS1)):
                pe.wait_ge(mlp_moved, m * STEPS + chunks[-1] + 1)
                for k in chunks:
                    last = pe.matmul(psM[c % 2][:, 0:SPAN], w2s[:, k, c * P:(c + 1) * P], h1[:, k, :],
                                     start=k == 0, stop=k == CHUNKS1 - 1)
                if k == CHUNKS1 - 1:
                    last.then_inc(mlp_ready, 1)

            def layer3(m):
                for k in range(CHUNKS2):
                    pe.wait_ge(mlp_moved, m * STEPS + CHUNKS1 + k + 1)
                    last = pe.matmul(psM[0][0:1, 0:SPAN], w3s[:, k:k + 1], h2[:, k, :],
                                     start=k == 0, stop=k == CHUNKS2 - 1)
                last.then_inc(mlp_ready, 1)

            pe.wait_ge(pick_ready, 1)
            pe.wait_ge(lids_taken, 1)
            spread_ids(0, 0, True)
            spread_ids(0, 1, True)
            look_up(0, 0, True)
            look_up(0, 1, True)
            spread_ids(0, 2)
            look_up(0, 2, True)
            look_up(0, 3, True)
            spread_ids(0, 3)
            pe.wait_ge(ident_ready, 1)
            transpose(0, 0, True)
            for t in range(HOTS, LOOKUPS):
                look_up(0, t, True)
            pe.wait_ge(lids_taken, 2)
            spread_ids(1, 0)
            spread_ids(1, 1)
            gram(0, 0, 0)
            gram(0, 0, 1)
            transpose(0, 1, True)
            gram(0, 1, 0)
            gram(0, 1, 1)
            spread_ids(1, 2)
            pe.wait_ge(item_low, ITEMS)
            pe.wait_ge(constants_in, 16 * 4)

            def turn_up_to_packs(turn, more):
                for t in range(HOTS - 1):
                    look_up(turn, t)
                spread_ids(turn, 3)
                look_up(turn, 3)
                transpose(turn, 0)
                look_up(turn, 4)
                look_up(turn, 5)
                layer1_high(turn - 1, 0)
                look_up(turn, 6)
                layer1_low(turn - 1, 0)
                if more:
                    pe.wait_ge(lids_taken, turn + 2)
                    spread_ids(turn + 1, 0)
                    spread_ids(turn + 1, 1)
                gram(turn, 0, 0)
                layer1(turn - 1, 1)
                gram(turn, 0, 1)
                layer1(turn - 1, 2)
                layer1(turn - 1, 3)
                transpose(turn, 1)

            with pe.Fori(1, TURNS - 1) as turn:
                turn_up_to_packs(turn, True)
                layer2(turn - 1, 0)
                spread_ids(turn + 1, 2)
                gram(turn, 1, 0)
                layer2(turn - 1, 1)
                gram(turn, 1, 1)
                layer3(turn - 1)

            last_turn = TURNS - 1
            turn_up_to_packs(last_turn, False)
            pe.wait_ge(mlp_moved, (last_turn - 1) * STEPS + CHUNKS1)
            layer2(last_turn - 1, 0, range(CHUNKS1 // 2))
            gram(last_turn, 1, 0)
            gram(last_turn, 1, 1)
            layer2(last_turn - 1, 0, range(CHUNKS1 // 2, CHUNKS1))
            layer2(last_turn - 1, 1)
            layer1_high(last_turn, 0, LAST_BANKS[0])
            layer3(last_turn - 1)
            layer1_low(last_turn, 0, LAST_BANKS[0])
            for c in range(1, CHUNKS1):
                layer1(last_turn, c, LAST_BANKS[c])
            pe.wait_ge(mlp_moved, last_turn * STEPS)
            for chunks in (range(CHUNKS1 - 1), range(CHUNKS1 - 1, CHUNKS1)):
                for c in range(CHUNKS2):
                    layer2(last_turn, c, chunks)
            layer3(last_turn)

        @block.vector
        def _(dve):
            def pack(turn, b, first=False):
                if not first:
                    dve.wait_ge(gram_moved, turn * 4 - 2 + 2 * b)
                for k in range(1, PACKS, 2):
                    n = pack_slots(k)
                    dve.wait_ge(pack_ready, turn * (2 * PACKS) + b * PACKS + k + 1)
                    dve.tensor_copy(vecT[:, b * P:(b + 1) * P, k * PACK:k * PACK + n],
                                    bank("pack", b, k)[:, 0:n * P].rearrange("d (s p) -> d p s", s=n))\
                       .then_inc(packs_moved[1], 1)

            def make_onehot(turn, t, first=False):
                dve.wait_ge(ids_spread, turn * COUPLES + t // 2 + 1)
                if not first:
                    dve.wait_ge(looked_up, turn * LOOKUPS + t + 1 - HOT_WAIT[t])
                for k in range(BLOCKS):
                    last = dve.tensor_scalar(onehot[t % HOTS][:, k, :],
                                             psI[(t // 2) % 2][0:BLOCK, (t % 2) * SPAN:(t % 2 + 1) * SPAN],
                                             row_number[0:BLOCK, k:k + 1], None, ALU.is_equal)
                last.then_inc(onehot_ready, 1)

            def spread_first_half(turn, b, done, first=False):
                if not first:
                    dve.wait_ge(terms_low_ready, turn * 2 + b)
                dve.wait_ge(gram_ready, turn * 4 + 2 * b + 1)
                spread_moves(dve.tensor_copy, 0, WHOLE_MOVES[:3]).then_inc(vector_whole_moved, 1)
                spread_moves(dve.tensor_copy, 0, WHOLE_MOVES[3:4])
                dve.wait_ge(vector_whole_moved, done)
                spread_moves(dve.tensor_copy, 0, TOP_MOVES).then_inc(vector_tops_moved, 1)
                spread_moves(dve.tensor_copy, 0, WHOLE_MOVES[4:])
                dve.wait_ge(vector_tops_moved, done)
                spread_moves(dve.tensor_copy, 0, [LAST_MOVE]).then_inc(gram_moved, 1)

            def low_item(n):
                raw, high, low = item(n)
                if n == ITEMS - 1:
                    dve.wait_ge(item_in[n], 2 * 16)
                    dve.tensor_tensor(w_dense[:, :], w_dense[:, :], w_places[COLS], ALU.add)\
                       .then_inc(w_dense_ready, 1)
                dve.wait_ge(item_high, n + 1)
                dve.tensor_tensor(low, raw, high.bitcast(fp32), ALU.subtract).then_inc(item_low, 1)

            def low_terms(tile, b):
                dve.wait_ge(terms_high_ready, tile + 1)
                at = slice(b * P, (b + 1) * P)
                dve.tensor_tensor(terms_low[:, :, at], terms[:, :, :], terms_high[:, :, at].bitcast(fp32),
                                  ALU.subtract).then_inc(terms_low_ready, 1)

            dve.wait_ge(ident_ready, 1)
            dve.tensor_copy(pick[:, :, :],
                            ident[0:LOOKUPS, 0:LOOKUPS].unsqueeze(2).to_broadcast([LOOKUPS, LOOKUPS, P]))\
               .then_inc(pick_ready, 1)
            dve.wait_ge(lids_in, 16)
            dve.tensor_copy(lidf[:, :], lids[:, :]).then_inc(lids_taken, 1)
            dve.wait_ge(row_number_ready, 1)
            make_onehot(0, 0, True)
            make_onehot(0, 1, True)
            low_item(0)
            low_item(1)
            make_onehot(0, 2, True)
            for t in range(2, LOOKUPS):
                low_item(t)
            make_onehot(0, 3, True)
            make_onehot(0, HOTS)
            pack(0, 0, True)
            for t in range(HOTS + 1, LOOKUPS):
                make_onehot(0, t)
            for n in range(LOOKUPS, ITEMS):
                low_item(n)
            dve.wait_ge(terms_zeroed, 1)
            spread_first_half(0, 0, 1, True)
            pack(0, 1, True)
            make_onehot(1, 0)
            low_terms(0, 0)
            make_onehot(1, 1)
            make_onehot(1, 2)
            make_onehot(1, 3)

            def one_turn(turn, more):
                make_onehot(turn, 4)
                make_onehot(turn, 5)
                pack(turn, 0)
                low_terms(turn * 2 - 1, 1)
                make_onehot(turn, 6)
                if more:
                    make_onehot(turn + 1, 0)
                    make_onehot(turn + 1, 1)
                    make_onehot(turn + 1, 2)
                pack(turn, 1)
                low_terms(turn * 2, 0)

            with dve.Fori(1, TURNS - 1) as turn:
                one_turn(turn, True)
                make_onehot(turn + 1, 3)
            one_turn(TURNS - 1, False)
            spread_first_half(TURNS - 1, 1, 2)
            low_terms(TURNS * 2 - 1, 1)

        @block.scalar
        def _(act):
            def take_lids(turn):
                act.wait_ge(lids_in, turn * 16 + 16)
                act.wait_ge(ids_spread, turn * COUPLES)
                act.activation(lidf[:, :], lids[:, :], ACT.Copy).then_inc(lids_taken, 1)

            def high_item(n):
                raw, high, _ = item(n)
                if n == ITEMS - 1:
                    act.wait_ge(w_dense_ready, 1)
                else:
                    act.wait_ge(item_in[n], 16)
                act.activation(high, raw, ACT.Copy).then_inc(item_high, 1)

            def move_lookup(turn, t):
                act.wait_ge(looked_up, turn * LOOKUPS + t + 1)
                act.activation(vecT[:, :, ROW_SLOTS + t], bank("lookup", t)[:, 0:SPAN], ACT.Copy)\
                   .then_inc(lookup_moved, 1)

            def pack(turn, b):
                def move(k, to):
                    n = pack_slots(k)
                    return act.activation(vecT[:, b * P:(b + 1) * P, to:to + n],
                                          bank("pack", b, k)[:, 0:n * P].rearrange("d (s p) -> d p s", s=n),
                                          ACT.Copy)

                for k in range(0, PACKS, 2):
                    act.wait_ge(pack_ready, turn * (2 * PACKS) + b * PACKS + k + 1)
                    if k == 0:
                        move(0, SLOTS)
                    move(k, k * PACK).then_inc(packs_moved[0], 1)

            def spread(turn, b, half, alone=True, first=False):
                if half == 0 or not alone:
                    if not first:
                        act.wait_ge(terms_low_ready, turn * 2 + b)
                    act.wait_ge(gram_ready, turn * 4 + 2 * b + 1)
                    act.activation(terms[:, COLS, :], vecT[:, b * P:(b + 1) * P, 0], ACT.Copy)
                act.wait_ge(gram_ready, turn * 4 + 2 * b + half + 1)

                def move(to, of):
                    return act.activation(to, of, ACT.Copy)

                done = turn * 4 + 2 * b + half - (0 if alone or first else 1)
                spread_moves(move, half, WHOLE_MOVES[:3]).then_inc(whole_moved, 1)
                spread_moves(move, half, WHOLE_MOVES[3:4])
                act.wait_ge(whole_moved, done)
                spread_moves(move, half, TOP_MOVES).then_inc(tops_moved, 1)
                spread_moves(move, half, WHOLE_MOVES[4:])
                act.wait_ge(tops_moved, done)
                if not alone:
                    act.wait_ge(gram_moved, turn * 4 + 2 * b + 1)
                spread_moves(move, half, [LAST_MOVE]).then_inc(gram_moved, 1)

            def high_terms(turn, b, first=False):
                act.wait_ge(gram_moved, turn * 4 + 2 * b + 2)
                if not first:
                    act.wait_ge(mlp_ready, (turn - 1) * STEPS + CHUNKS1)
                act.activation(terms_high[:, :, b * P:(b + 1) * P], terms[:, :, :], ACT.Copy)\
                   .then_inc(terms_high_ready, 1)

            def relu1(m, c, bank=None):
                act.wait_ge(mlp_ready, m * STEPS + c + 1)
                o = psM[c % 2] if bank is None else bank
                act.activation(h1[:, c, :], o[:, 0:SPAN], ACT.Relu, bias=b1s[:, c:c + 1])\
                   .then_inc(mlp_moved, 1)

            def relu2(m, c):
                act.wait_ge(mlp_ready, m * STEPS + CHUNKS1 + c + 1)
                act.activation(h2[:, c, :], psM[c % 2][:, 0:SPAN], ACT.Relu, bias=b2s[:, c:c + 1])\
                   .then_inc(mlp_moved, 1)

            def store_y(m):
                act.wait_ge(mlp_ready, m * STEPS + STEPS)
                act.wait_ge(y_stored, m * 16 + 16)
                act.activation(y[:, :], psM[0][0:1, 0:SPAN], ACT.Copy).then_inc(mlp_moved, 1)
                act.wait_ge(mlp_moved, m * STEPS + STEPS)
                act.dma_start(out[:, bass.ds(m * SPAN, SPAN)], y[:, :]).then_inc(y_stored, 16)

            act.sem_inc(y_stored, 16)
            act.dma_start(w3s[:, :], w3).then_inc(constants_in, 16)
            act.dma_start(b1s[:, :], b1).then_inc(constants_in, 16)
            act.dma_start(b2s[:, :], b2).then_inc(constants_in, 16)
            act.dma_start(w2s[:, :, :], w2.rearrange("(k p) n -> p k n", p=P)).then_inc(constants_in, 16)
            for n in range(LOOKUPS):
                high_item(n)
            act.wait_ge(item_low, LOOKUPS)
            for t in range(HOTS):
                move_lookup(0, t)
            take_lids(1)
            pack(0, 0)
            move_lookup(0, 4)
            for n in range(LOOKUPS, LOOKUPS + 3):
                high_item(n)
            move_lookup(0, 5)
            for n in range(LOOKUPS + 3, LOOKUPS + 5):
                high_item(n)
            move_lookup(0, 6)
            for n in range(LOOKUPS + 5, ITEMS):
                high_item(n)
            act.wait_ge(constants_in, 16 * 4)
            act.wait_ge(terms_zeroed, 1)
            spread(0, 0, 1, alone=False, first=True)
            pack(0, 1)
            high_terms(0, 0, True)
            spread(0, 1, 0)
            spread(0, 1, 1)
            high_terms(0, 1, True)

            def turn_up_to_packs(turn, more):
                pack(turn, 0)
                move_lookup(turn, 4)
                if more:
                    take_lids(turn + 1)
                move_lookup(turn, 5)
                move_lookup(turn, 6)
                relu1(turn - 1, 0)
                spread(turn, 0, 0)
                relu1(turn - 1, 1)
                spread(turn, 0, 1)
                relu1(turn - 1, 2)
                relu1(turn - 1, 3)
                pack(turn, 1)
                high_terms(turn, 0)

            for t in range(HOTS):
                move_lookup(1, t)
            with act.Fori(1, TURNS - 1) as turn:
                turn_up_to_packs(turn, True)
                relu2(turn - 1, 0)
                spread(turn, 1, 0)
                relu2(turn - 1, 1)
                spread(turn, 1, 1)
                move_lookup(turn + 1, 0)
                high_terms(turn, 1)
                store_y(turn - 1)
                for t in range(1, HOTS):
                    move_lookup(turn + 1, t)
            last_turn = TURNS - 1
            turn_up_to_packs(last_turn, False)
            spread(last_turn, 1, 1, alone=False)
            high_terms(last_turn, 1)
            for c in range(CHUNKS2):
                relu2(last_turn - 1, c)
            store_y(last_turn - 1)
            for c in range(CHUNKS1):
                relu1(last_turn, c, LAST_BANKS[c])
            for c in range(CHUNKS2):
                relu2(last_turn, c)
            store_y(last_turn)
            act.wait_ge(y_stored, 16 * (TURNS + 1))


def kernel(**inputs):
    import numpy as np
    import concourse.bacc as bacc
    from concourse.bass_utils import run_bass_kernel_spmd

    nc = bacc.Bacc("TRN2", target_bir_lowering=False, num_devices=1)
    arrays = {}

    def give(name, a):
        a = np.ascontiguousarray(a)
        arrays[name] = a
        return nc.dram_tensor(name, a.shape, mybir.dt.from_np(a.dtype), kind="ExternalInput").ap()

    vector_of_slot = [0] + [1 + t for t in GATHER_TABLES + LOOKUP_TABLES]
    w1 = np.asarray(inputs["W_top1"])
    n_pairs = SLOTS * (SLOTS - 1) // 2
    row_of_pair = {}
    for f in range(SLOTS):
        for g in range(f + 1, SLOTS):
            row_of_pair[f, g] = D + len(row_of_pair)
    w_terms = np.zeros((P, COLS + 2, HIDDEN1), w1.dtype)
    for (f, g), (partition, column) in pair_places().items():
        u, v = sorted((vector_of_slot[f], vector_of_slot[g]))
        w_terms[partition, column] = w1[row_of_pair[u, v]]
    w_terms[:, COLS] = w1[:D]
    w_terms[:, COLS + 1] = w1[D + n_pairs:]
    ids = np.asarray(inputs["ids"])
    out = nc.dram_tensor("y_out", (1, BATCH), mybir.dt.float32, kind="ExternalOutput").ap()
    build(nc,
          give("dense", inputs["r_dense_features"]), give("ids", ids),
          give("lookup_ids", ids[:, LOOKUP_TABLES].T),
          [give(f"tbl_{t}", inputs[f"tbl_{t}"]) for t in GATHER_TABLES],
          [give(f"tbl_{t}", inputs[f"tbl_{t}"]) for t in LOOKUP_TABLES],
          give("w_terms", w_terms),
          give("b1", np.asarray(inputs["b_top1"]).reshape(CHUNKS1, P).T),
          give("w2", inputs["W_top2"]),
          give("b2", np.asarray(inputs["b_top2"]).reshape(CHUNKS2, P).T),
          give("w3", np.asarray(inputs["W_top3"]).reshape(CHUNKS2, P).T),
          out)
    r = run_bass_kernel_spmd(nc, [arrays], core_ids=[0])
    return r.results[0]["y_out"].reshape(BATCH, 1)
```
